# Optimizing a Trainium2 kernel written in Bass

```python
import numpy as np
import jax
import jax.numpy as jnp

def _softmax(x, axis=-1):
    return jax.nn.softmax(x, axis=axis)

def _gelu(x):
    return jax.nn.gelu(x, approximate=True)

def _silu(x):
    return jax.nn.silu(x)

def _sigmoid(x):
    return jax.nn.sigmoid(x)

def _layernorm(x, axis=-1, eps=1e-05):
    m = jnp.mean(x, axis=axis, keepdims=True)
    v = jnp.var(x, axis=axis, keepdims=True)
    return (x - m) / jnp.sqrt(v + eps)

def _scatter_add(tgt, idx, src, axis=0):
    return tgt.at[idx].add(src)

def _segment_sum(src, seg, n):
    return jax.ops.segment_sum(src, seg, n)
kernel_name = 'mk_dlrm_tower_d1_rec_r8_8b2009'

def setup_inputs(seed: int=0):
    np.random.seed(seed)
    _w = jnp.asarray

    def _rec_inputs():
        import jax
        import jax.numpy as jnp
        _tk = jax.random.key(seed)
        dense_ctx = jax.random.normal(jax.random.fold_in(_tk, 190), (2048, 16), jnp.float32)
        ids = jnp.stack([jax.random.randint(jax.random.fold_in(_tk, 200 + f), (2048,), 0, v, jnp.int32) for f, v in enumerate([12500, 1000, 1000, 125000, 12500, 125000, 1250, 1000, 1000, 1000, 125000, 1250, 1250, 1250, 1000, 1000, 1000, 1250, 1250, 12500, 1250, 1250, 1000, 1000, 1250, 1250, 1000, 12500, 1250, 1000, 1250, 12500, 12500, 1250, 1250, 12500, 1000, 1000, 1250])], axis=1)
        tbl_0 = 0.05 * jax.random.normal(jax.random.fold_in(_tk, 500 + 0), (12500, 64), jnp.float32)
        tbl_1 = 0.05 * jax.random.normal(jax.random.fold_in(_tk, 500 + 1), (1000, 64), jnp.float32)
        tbl_2 = 0.05 * jax.random.normal(jax.random.fold_in(_tk, 500 + 2), (1000, 64), jnp.float32)
        tbl_3 = 0.05 * jax.random.normal(jax.random.fold_in(_tk, 500 + 3), (125000, 64), jnp.float32)
        tbl_4 = 0.05 * jax.random.normal(jax.random.fold_in(_tk, 500 + 4), (12500, 64), jnp.float32)
        tbl_5 = 0.05 * jax.random.normal(jax.random.fold_in(_tk, 500 + 5), (125000, 64), jnp.float32)
        tbl_6 = 0.05 * jax.random.normal(jax.random.fold_in(_tk, 500 + 6), (1250, 64), jnp.float32)
        tbl_7 = 0.05 * jax.random.normal(jax.random.fold_in(_tk, 500 + 7), (1000, 64), jnp.float32)
        tbl_8 = 0.05 * jax.random.normal(jax.random.fold_in(_tk, 500 + 8), (1000, 64), jnp.float32)
        tbl_9 = 0.05 * jax.random.normal(jax.random.fold_in(_tk, 500 + 9), (1000, 64), jnp.float32)
        tbl_10 = 0.05 * jax.random.normal(jax.random.fold_in(_tk, 500 + 10), (125000, 64), jnp.float32)
        tbl_11 = 0.05 * jax.random.normal(jax.random.fold_in(_tk, 500 + 11), (1250, 64), jnp.float32)
        tbl_12 = 0.05 * jax.random.normal(jax.random.fold_in(_tk, 500 + 12), (1250, 64), jnp.float32)
        tbl_13 = 0.05 * jax.random.normal(jax.random.fold_in(_tk, 500 + 13), (1250, 64), jnp.float32)
        tbl_14 = 0.05 * jax.random.normal(jax.random.fold_in(_tk, 500 + 14), (1000, 64), jnp.float32)
        tbl_15 = 0.05 * jax.random.normal(jax.random.fold_in(_tk, 500 + 15), (1000, 64), jnp.float32)
        tbl_16 = 0.05 * jax.random.normal(jax.random.fold_in(_tk, 500 + 16), (1000, 64), jnp.float32)
        tbl_17 = 0.05 * jax.random.normal(jax.random.fold_in(_tk, 500 + 17), (1250, 64), jnp.float32)
        tbl_18 = 0.05 * jax.random.normal(jax.random.fold_in(_tk, 500 + 18), (1250, 64), jnp.float32)
        tbl_19 = 0.05 * jax.random.normal(jax.random.fold_in(_tk, 500 + 19), (12500, 64), jnp.float32)
        tbl_20 = 0.05 * jax.random.normal(jax.random.fold_in(_tk, 500 + 20), (1250, 64), jnp.float32)
        tbl_21 = 0.05 * jax.random.normal(jax.random.fold_in(_tk, 500 + 21), (1250, 64), jnp.float32)
        tbl_22 = 0.05 * jax.random.normal(jax.random.fold_in(_tk, 500 + 22), (1000, 64), jnp.float32)
        tbl_23 = 0.05 * jax.random.normal(jax.random.fold_in(_tk, 500 + 23), (1000, 64), jnp.float32)
        tbl_24 = 0.05 * jax.random.normal(jax.random.fold_in(_tk, 500 + 24), (1250, 64), jnp.float32)
        tbl_25 = 0.05 * jax.random.normal(jax.random.fold_in(_tk, 500 + 25), (1250, 64), jnp.float32)
        tbl_26 = 0.05 * jax.random.normal(jax.random.fold_in(_tk, 500 + 26), (1000, 64), jnp.float32)
        tbl_27 = 0.05 * jax.random.normal(jax.random.fold_in(_tk, 500 + 27), (12500, 64), jnp.float32)
        tbl_28 = 0.05 * jax.random.normal(jax.random.fold_in(_tk, 500 + 28), (1250, 64), jnp.float32)
        tbl_29 = 0.05 * jax.random.normal(jax.random.fold_in(_tk, 500 + 29), (1000, 64), jnp.float32)
        tbl_30 = 0.05 * jax.random.normal(jax.random.fold_in(_tk, 500 + 30), (1250, 64), jnp.float32)
        tbl_31 = 0.05 * jax.random.normal(jax.random.fold_in(_tk, 500 + 31), (12500, 64), jnp.float32)
        tbl_32 = 0.05 * jax.random.normal(jax.random.fold_in(_tk, 500 + 32), (12500, 64), jnp.float32)
        tbl_33 = 0.05 * jax.random.normal(jax.random.fold_in(_tk, 500 + 33), (1250, 64), jnp.float32)
        tbl_34 = 0.05 * jax.random.normal(jax.random.fold_in(_tk, 500 + 34), (1250, 64), jnp.float32)
        tbl_35 = 0.05 * jax.random.normal(jax.random.fold_in(_tk, 500 + 35), (12500, 64), jnp.float32)
        tbl_36 = 0.05 * jax.random.normal(jax.random.fold_in(_tk, 500 + 36), (1000, 64), jnp.float32)
        tbl_37 = 0.05 * jax.random.normal(jax.random.fold_in(_tk, 500 + 37), (1000, 64), jnp.float32)
        tbl_38 = 0.05 * jax.random.normal(jax.random.fold_in(_tk, 500 + 38), (1250, 64), jnp.float32)
        _rk = jax.random.fold_in(_tk, 7)
        W_top1 = 0.0833333 * jax.random.normal(jax.random.fold_in(_tk, 801), (144, 512), jnp.float32)
        W_top2 = 0.0441942 * jax.random.normal(jax.random.fold_in(_tk, 802), (512, 256), jnp.float32)
        W_top3 = 0.0625 * jax.random.normal(jax.random.fold_in(_tk, 803), (256, 1), jnp.float32)
        b_top1 = jnp.zeros((512,), jnp.float32)
        b_top2 = jnp.zeros((256,), jnp.float32)
        return (dense_ctx, ids, tbl_0, tbl_1, tbl_2, tbl_3, tbl_4, tbl_5, tbl_6, tbl_7, tbl_8, tbl_9, tbl_10, tbl_11, tbl_12, tbl_13, tbl_14, tbl_15, tbl_16, tbl_17, tbl_18, tbl_19, tbl_20, tbl_21, tbl_22, tbl_23, tbl_24, tbl_25, tbl_26, tbl_27, tbl_28, tbl_29, tbl_30, tbl_31, tbl_32, tbl_33, tbl_34, tbl_35, tbl_36, tbl_37, tbl_38, W_top1, b_top1, W_top2, b_top2, W_top3)
    dense_ctx, ids, tbl_0, tbl_1, tbl_2, tbl_3, tbl_4, tbl_5, tbl_6, tbl_7, tbl_8, tbl_9, tbl_10, tbl_11, tbl_12, tbl_13, tbl_14, tbl_15, tbl_16, tbl_17, tbl_18, tbl_19, tbl_20, tbl_21, tbl_22, tbl_23, tbl_24, tbl_25, tbl_26, tbl_27, tbl_28, tbl_29, tbl_30, tbl_31, tbl_32, tbl_33, tbl_34, tbl_35, tbl_36, tbl_37, tbl_38, W_top1, b_top1, W_top2, b_top2, W_top3 = _rec_inputs()

    def _L0_rec_setup():
        import jax, jax.numpy as jnp
        import numpy as np
        B, F, E, UNITS = (1024, 39, 64, 128)
        key = jax.random.key(seed)
        k1, k2 = jax.random.split(key)
        embeds = jax.random.normal(k1, (B, F, E), dtype=jnp.float32)
        inner_w = jax.random.normal(k2, (UNITS, F), dtype=jnp.float32) * (2.0 / (UNITS + F)) ** 0.5
        return {'embeds': embeds, 'inner_w': inner_w}
    _L0_rec_all = _L0_rec_setup()
    _L0_rec_in = {k: v for k, v in _L0_rec_all.items() if k in ('inner_w',)}
    del _L0_rec_all
    return {'dense_ctx': dense_ctx, 'ids': ids, 'tbl_0': tbl_0, 'tbl_1': tbl_1, 'tbl_2': tbl_2, 'tbl_3': tbl_3, 'tbl_4': tbl_4, 'tbl_5': tbl_5, 'tbl_6': tbl_6, 'tbl_7': tbl_7, 'tbl_8': tbl_8, 'tbl_9': tbl_9, 'tbl_10': tbl_10, 'tbl_11': tbl_11, 'tbl_12': tbl_12, 'tbl_13': tbl_13, 'tbl_14': tbl_14, 'tbl_15': tbl_15, 'tbl_16': tbl_16, 'tbl_17': tbl_17, 'tbl_18': tbl_18, 'tbl_19': tbl_19, 'tbl_20': tbl_20, 'tbl_21': tbl_21, 'tbl_22': tbl_22, 'tbl_23': tbl_23, 'tbl_24': tbl_24, 'tbl_25': tbl_25, 'tbl_26': tbl_26, 'tbl_27': tbl_27, 'tbl_28': tbl_28, 'tbl_29': tbl_29, 'tbl_30': tbl_30, 'tbl_31': tbl_31, 'tbl_32': tbl_32, 'tbl_33': tbl_33, 'tbl_34': tbl_34, 'tbl_35': tbl_35, 'tbl_36': tbl_36, 'tbl_37': tbl_37, 'tbl_38': tbl_38, 'W_top1': W_top1, 'b_top1': b_top1, 'W_top2': W_top2, 'b_top2': b_top2, 'W_top3': W_top3, 'L0_rec_inner_w': _L0_rec_in['inner_w']}

def reference(dense_ctx, ids, tbl_0, tbl_1, tbl_2, tbl_3, tbl_4, tbl_5, tbl_6, tbl_7, tbl_8, tbl_9, tbl_10, tbl_11, tbl_12, tbl_13, tbl_14, tbl_15, tbl_16, tbl_17, tbl_18, tbl_19, tbl_20, tbl_21, tbl_22, tbl_23, tbl_24, tbl_25, tbl_26, tbl_27, tbl_28, tbl_29, tbl_30, tbl_31, tbl_32, tbl_33, tbl_34, tbl_35, tbl_36, tbl_37, tbl_38, W_top1, b_top1, W_top2, b_top2, W_top3, L0_rec_inner_w):
    import jax
    import jax.numpy as jnp

    def _L0_rec_ref(embeds, inner_w):
        import jax, jax.numpy as jnp
        import numpy as np
        B, F, E, UNITS = (1024, 39, 64, 128)
        delta = jnp.einsum('uf,bfe->bue', inner_w, embeds)
        lp = jnp.sum(delta * delta, axis=-1)
        return lp
    e = jnp.stack([tbl_0[ids[:, 0]], tbl_1[ids[:, 1]], tbl_2[ids[:, 2]], tbl_3[ids[:, 3]], tbl_4[ids[:, 4]], tbl_5[ids[:, 5]], tbl_6[ids[:, 6]], tbl_7[ids[:, 7]], tbl_8[ids[:, 8]], tbl_9[ids[:, 9]], tbl_10[ids[:, 10]], tbl_11[ids[:, 11]], tbl_12[ids[:, 12]], tbl_13[ids[:, 13]], tbl_14[ids[:, 14]], tbl_15[ids[:, 15]], tbl_16[ids[:, 16]], tbl_17[ids[:, 17]], tbl_18[ids[:, 18]], tbl_19[ids[:, 19]], tbl_20[ids[:, 20]], tbl_21[ids[:, 21]], tbl_22[ids[:, 22]], tbl_23[ids[:, 23]], tbl_24[ids[:, 24]], tbl_25[ids[:, 25]], tbl_26[ids[:, 26]], tbl_27[ids[:, 27]], tbl_28[ids[:, 28]], tbl_29[ids[:, 29]], tbl_30[ids[:, 30]], tbl_31[ids[:, 31]], tbl_32[ids[:, 32]], tbl_33[ids[:, 33]], tbl_34[ids[:, 34]], tbl_35[ids[:, 35]], tbl_36[ids[:, 36]], tbl_37[ids[:, 37]], tbl_38[ids[:, 38]]], axis=1)
    z = _L0_rec_ref(e, L0_rec_inner_w)
    z = z.reshape(z.shape[0], -1)
    h = jnp.concatenate([z, dense_ctx], axis=1)
    h = jnp.maximum(h @ W_top1 + b_top1, 0.0)
    h = jnp.maximum(h @ W_top2 + b_top2, 0.0)
    y = h @ W_top3
    return y

_drawn_inputs = setup_inputs


def setup_inputs(seed=0):
    import zlib

    import numpy as np

    out = dict(_drawn_inputs(seed))
    spreads = {'b_top1': (0.0, 0.337), 'b_top2': (0.0, 0.1)}
    factors = {'tbl_0': 7.657,
     'tbl_1': 6.42,
     'tbl_2': 7.14,
     'tbl_3': 8.0,
     'tbl_4': 6.407,
     'tbl_5': 7.688,
     'tbl_6': 6.672,
     'tbl_7': 6.667,
     'tbl_8': 6.677,
     'tbl_9': 7.169,
     'tbl_10': 6.587,
     'tbl_11': 7.691,
     'tbl_12': 7.547,
     'tbl_13': 8.0,
     'tbl_14': 7.04,
     'tbl_15': 6.034,
     'tbl_16': 5.949,
     'tbl_17': 7.43,
     'tbl_18': 6.711,
     'tbl_19': 7.998,
     'tbl_20': 6.522,
     'tbl_21': 7.546,
     'tbl_22': 6.41,
     'tbl_23': 6.793,
     'tbl_24': 6.707,
     'tbl_25': 7.48,
     'tbl_26': 6.43,
     'tbl_27': 5.898,
     'tbl_28': 7.957,
     'tbl_29': 6.63,
     'tbl_30': 8.0,
     'tbl_31': 6.966,
     'tbl_32': 6.996,
     'tbl_33': 7.127,
     'tbl_34': 6.419,
     'tbl_35': 7.404,
     'tbl_36': 6.649,
     'tbl_37': 7.746,
     'tbl_38': 7.646}
    for name, (base, spread) in spreads.items():
        noise = np.random.default_rng([zlib.crc32(name.encode()), seed]).standard_normal(out[name].shape)
        drawn = base * np.exp(spread * noise) if base else spread * noise
        out[name] = jnp.asarray(drawn.astype(out[name].dtype))
    for name, factor in factors.items():
        out[name] = (out[name] * factor).astype(out[name].dtype)
    return out
```

```python
from contextlib import ExitStack

import concourse.bass as bass
from concourse import mybir

F32 = mybir.dt.float32
BF16 = mybir.dt.bfloat16
I32 = mybir.dt.int32
ALU = mybir.AluOpType
ACT = mybir.ActivationFunctionType
AX = mybir.AxisListType

P = 128
PARTS = 3
BANK = 512
CHUNK_E = 8
HALVES = 2


def dlrm_tower(nc, ids, tables, w_inner, dense, w1z, w1d, b1, w2, b2, w3, out):
    B, F = ids.shape
    E = tables[0].shape[1]
    U = w_inner.shape[1]
    KD = dense.shape[0]
    H1 = w1z.shape[1]
    H2 = w2.shape[1]
    M1, M2 = H1 // P, H2 // P
    PAIRS = B // (2 * P)
    PB = 2 * P
    K = PARTS * F
    CHUNKS = E // CHUNK_E
    CCOLS = CHUNK_E * P
    CH = CHUNKS // HALVES
    EH = E // HALVES
    assert U == P and K <= P and B % PB == 0 and M1 * PB == 2 * BANK and M2 * PB == BANK

    with ExitStack() as ctx:
        def sb(name, shape, dt):
            return ctx.enter_context(nc.sbuf_tensor(name, shape, dt))

        def sem(name):
            return ctx.enter_context(nc.semaphore(name))

        def sems(name):
            return [sem(f"{name}{k}") for k in range(2)]

        idx = sb("idx", [P, 2, F], I32)
        emb = sb("emb", [P, 2, F, E], F32)
        split = sb("split", [P, 2, E, P], BF16)
        moved = sb("moved", [P, 2, E, P], BF16)
        squares = sb("squares", [U, HALVES, EH, P], F32)
        half_sums = sb("half_sums", [U, HALVES, P], F32)
        z = sb("z", [U, PB], F32)
        w_rep = sb("w_rep", [K, U], F32)
        w_parts = sb("w_parts", [K, PARTS, U], BF16)
        w1z_sb = sb("w1z_sb", [U, H1], F32)
        w1d_sb = sb("w1d_sb", [KD, H1], F32)
        w2_sb = sb("w2_sb", [P, M1, H2], F32)
        w3_sb = sb("w3_sb", [P, M2], F32)
        b1_sb = sb("b1_sb", [P, M1], F32)
        b2_sb = sb("b2_sb", [P, M2], F32)
        dense_sb = sb("dense_sb", [KD, B], F32)
        h1 = sb("h1", [P, M1, PB], F32)
        h2 = sb("h2", [P, M2, PB], F32)
        y_sb = sb("y_sb", [1, B], F32)

        delta = ctx.enter_context(nc.psum_tensor("delta", [P, 2, CCOLS], F32))
        hid = ctx.enter_context(nc.psum_tensor("hid", [P, 2 * BANK], F32))
        hid2 = ctx.enter_context(nc.psum_tensor("hid2", [P, BANK], F32))
        yps = ctx.enter_context(nc.psum_tensor("yps", [P, BANK], F32))

        ids_ready = sems("ids_ready")
        gathered = sems("gathered")
        transposed = sems("transposed")
        pad_zero = sem("pad_zero")
        w_loaded = sem("w_loaded")
        mlp_loaded = sem("mlp_loaded")
        w_step = sem("w_step")
        high_ready = sem("high_ready")
        rest_ready = sem("rest_ready")
        mid_ready = sem("mid_ready")
        low_ready = sem("low_ready")
        delta_ready = sem("delta_ready")
        squared = sem("squared")
        reduced = sem("reduced")
        z_ready = sem("z_ready")
        hid1_ready = sem("hid1_ready")
        h1_ready = sem("h1_ready")
        hid2_ready = sem("hid2_ready")
        h2_ready = sem("h2_ready")
        y_ready = sem("y_ready")
        y_copied = sem("y_copied")
        stored = sem("stored")
        gather_gate = sem("gather_gate")
        transpose_gate = sem("transpose_gate")

        W_LOADS = PARTS
        MLP_LOADS = 7

        block = ctx.enter_context(nc.Block())

        @block.sync
        def _(sp):
            def load_ids(q, k):
                sp.dma_start(idx[:, k, :], ids[bass.ds(q * PB + k * P, P), :]).then_inc(ids_ready[k], 16)

            def transpose_tile(q, k, first=False):
                if not first:
                    sp.wait_ge(delta_ready, (2 * q + k - 1) * CHUNKS)
                    sp.sem_inc(transpose_gate, 1)
                sp.wait_ge(low_ready, 2 * q + k + 1)
                sp.sem_inc(transpose_gate, 1)
                sp.dma_start_transpose(moved[:, k, :, :], split[:, k, :, :].rearrange("b e r -> b (e r)")
                                       ).then_inc(transposed[k], 16)

            load_ids(0, 0)
            load_ids(0, 1)
            for n in range(PARTS):
                sp.dma_start(w_rep[n * F:(n + 1) * F, :], w_inner).then_inc(w_loaded, 16)
            for dst, src in ((w1z_sb[:], w1z), (w1d_sb[:], w1d), (w2_sb[:], w2.rearrange("(k p) n -> p k n", p=P)),
                             (w3_sb[:], w3), (b1_sb[:], b1), (b2_sb[:], b2),
                             (dense_sb[:], dense)):
                sp.dma_start(dst, src).then_inc(mlp_loaded, 16)
            sp.wait_ge(pad_zero, 1)

            def step(q, first=False):
                for k in range(2):
                    sp.wait_ge(gathered[k], (q + 1) * (16 * F))
                    sp.sem_inc(transpose_gate, 1)
                    load_ids(q + 1, k)
                    transpose_tile(q, k, first)

            step(0, first=True)
            with sp.Fori(1, PAIRS - 1) as q:
                step(q)
            for k in range(2):
                transpose_tile(PAIRS - 1, k)
            sp.wait_ge(y_copied, PAIRS)
            sp.dma_start(out.rearrange("b n -> n b"), y_sb[:]).then_inc(stored, 16)
            sp.wait_ge(stored, 16)

        @block.gpsimd
        def _(pool):
            def gather_pair(q, first=False):
                for k in range(2):
                    pool.wait_ge(ids_ready[k], q * 16 + 16)
                    if not first:
                        pool.wait_ge(low_ready, 2 * q + k - 1)
                        pool.sem_inc(gather_gate, 1)
                    for f in range(F):
                        nc.gpsimd.indirect_dma_start(
                            emb[:, k, f, :], None, tables[f][:],
                            bass.IndirectOffsetOnAxis(ap=idx[:, k, f:f + 1], axis=0)).then_inc(gathered[k], 16)

            gather_pair(0, first=True)
            with pool.Fori(1, PAIRS) as q:
                gather_pair(q)

        def rows(k, part):
            return split[:, k, :, part * F:(part + 1) * F].rearrange("b e f -> b f e")

        @block.scalar
        def _(act):
            def split_high_mid(q, k, first=False):
                act.wait_ge(gathered[k], q * (16 * F) + 16 * F)
                if not first:
                    act.wait_ge(transposed[k], q * 16)
                nc.scalar.copy(rows(k, 0), emb[:, k, :, :]).then_inc(high_ready, 1)
                act.wait_ge(rest_ready, 2 * q + k + 1)
                nc.scalar.copy(rows(k, 1), emb[:, k, :, :]).then_inc(mid_ready, 1)

            def square(q, k, c, first=False):
                n = q * (2 * CHUNKS) + k * CHUNKS + c
                act.wait_ge(delta_ready, n + 1)
                if c % CH == 0 and not (first and k == 0):
                    act.wait_ge(reduced, q * 4 + 2 * k + c // CH - 1)
                e0 = c % CH * CHUNK_E
                nc.scalar.activation(squares[:, c // CH, e0:e0 + CHUNK_E, :].rearrange("u e b -> u (e b)"),
                                     delta[:, c % 2, :], ACT.Square).then_inc(squared, 1)

            def mlp(q):
                act.wait_ge(hid1_ready, q + 1)
                for m in range(M1):
                    nc.scalar.activation(h1[:, m, :], hid[:, m * PB:(m + 1) * PB], ACT.Relu,
                                         bias=b1_sb[:, m:m + 1]).then_inc(h1_ready, 1)
                act.wait_ge(hid2_ready, q + 1)
                for m in range(M2):
                    nc.scalar.activation(h2[:, m, :], hid2[:, m * PB:(m + 1) * PB], ACT.Relu,
                                         bias=b2_sb[:, m:m + 1]).then_inc(h2_ready, 1)
                act.wait_ge(y_ready, q + 1)
                nc.scalar.copy(y_sb[:, bass.ds(q * PB, PB)], yps[0:1, 0:PB]).then_inc(y_copied, 1)

            def step(q, first=False, last=False):
                for k in range(2):
                    for c in range(CHUNKS):
                        square(q, k, c, first)
                        if not first and k == 0 and c == CH - 1:
                            mlp(q - 1)
                    if not last:
                        split_high_mid(q + 1, k)

            act.wait_ge(pad_zero, 1)
            for k in range(2):
                split_high_mid(0, k, first=True)
            act.wait_ge(mlp_loaded, 16 * MLP_LOADS)
            step(0, first=True)
            with act.Fori(1, PAIRS - 1) as q:
                step(q)
            step(PAIRS - 1, last=True)
            mlp(PAIRS - 1)

        @block.vector
        def _(dve):
            def split_rest_low(q, k):
                dve.wait_ge(high_ready, 2 * q + k + 1)
                nc.vector.tensor_tensor(emb[:, k, :, :], emb[:, k, :, :], rows(k, 0),
                                        ALU.subtract).then_inc(rest_ready, 1)
                dve.wait_ge(mid_ready, 2 * q + k + 1)
                nc.vector.tensor_tensor(rows(k, 2), emb[:, k, :, :], rows(k, 1),
                                        ALU.subtract).then_inc(low_ready, 1)

            def reduce_tile(q, k, first=False):
                if not (first and k == 0):
                    dve.wait_ge(z_ready, 2 * q + k)
                for h in range(HALVES):
                    dve.wait_ge(squared, q * (2 * CHUNKS) + k * CHUNKS + (h + 1) * CH)
                    nc.vector.tensor_reduce(half_sums[:, h, :], squares[:, h, :, :].rearrange("u e b -> u b e"),
                                            AX.X, ALU.add).then_inc(reduced, 1)
                dve.wait_ge(reduced, q * 4 + 2 * k + 2)
                if not first and k == 0:
                    dve.wait_ge(hid1_ready, q)
                nc.vector.tensor_tensor(z[:, k * P:(k + 1) * P], half_sums[:, 0, :], half_sums[:, 1, :],
                                        ALU.add).then_inc(z_ready, 1)

            nc.vector.memset(split[:, :, :, K:P], 0.0).then_inc(pad_zero, 1)
            dve.wait_ge(w_loaded, 16 * W_LOADS)
            done = 0
            for n in range(PARTS):
                nc.vector.tensor_copy(w_parts[:, n, :], w_rep[:]).then_inc(w_step, 1)
                done += 1
                if n < PARTS - 1:
                    dve.wait_ge(w_step, done)
                    nc.vector.tensor_tensor(w_rep[:], w_rep[:], w_parts[:, n, :], ALU.subtract).then_inc(w_step, 1)
                    done += 1
                    dve.wait_ge(w_step, done)
            for k in range(2):
                split_rest_low(0, k)
            for k in range(2):
                reduce_tile(0, k, first=True)
                split_rest_low(1, k)
            with dve.Fori(1, PAIRS - 1) as q:
                for k in range(2):
                    reduce_tile(q, k)
                    split_rest_low(q + 1, k)
            for k in range(2):
                reduce_tile(PAIRS - 1, k)

        @block.tensor
        def _(pe):
            def product(q, k, c, first=False):
                n = q * (2 * CHUNKS) + k * CHUNKS + c
                if not (first and k == 0 and c < 2):
                    pe.wait_ge(squared, n - 1)
                for part in range(PARTS):
                    for h in range(CCOLS // BANK):
                        e0 = c * CHUNK_E + h * (BANK // P)
                        last = nc.tensor.matmul(delta[:, c % 2, h * BANK:(h + 1) * BANK], w_parts[:, part, :],
                                                moved[0:K, k, e0:e0 + BANK // P, :].rearrange("r e b -> r (e b)"),
                                                start=(part == 0), stop=(part == PARTS - 1))
                last.then_inc(delta_ready, 1)

            def mlp(q):
                pe.wait_ge(z_ready, 2 * q + 2)
                for m in range(M1):
                    o = hid[:, m * PB:(m + 1) * PB]
                    nc.tensor.matmul(o, w1z_sb[:, m * P:(m + 1) * P], z[:], start=True, stop=False)
                    last = nc.tensor.matmul(o, w1d_sb[:, m * P:(m + 1) * P], dense_sb[:, bass.ds(q * PB, PB)],
                                            start=False, stop=True)
                last.then_inc(hid1_ready, 1)
                pe.wait_ge(h1_ready, q * M1 + M1)
                for m in range(M2):
                    for j in range(M1):
                        last = nc.tensor.matmul(hid2[:, m * PB:(m + 1) * PB], w2_sb[:, j, m * P:(m + 1) * P],
                                                h1[:, j, :], start=(j == 0), stop=(j == M1 - 1))
                last.then_inc(hid2_ready, 1)
                pe.wait_ge(h2_ready, q * M2 + M2)
                for j in range(M2):
                    last = nc.tensor.matmul(yps[0:1, 0:PB], w3_sb[:, j:j + 1], h2[:, j, :],
                                            start=(j == 0), stop=(j == M2 - 1))
                last.then_inc(y_ready, 1)

            def step(q, first=False):
                for k in range(2):
                    pe.wait_ge(transposed[k], q * 16 + 16)
                    for c in range(CHUNKS):
                        product(q, k, c, first)
                        if not first and k == 0 and c == CH - 1:
                            mlp(q - 1)

            pe.wait_ge(w_step, 2 * PARTS - 1)
            pe.wait_ge(mlp_loaded, 16 * MLP_LOADS)
            step(0, first=True)
            with pe.Fori(1, PAIRS) as q:
                step(q)
            mlp(PAIRS - 1)


def kernel(**inputs):
    import numpy as np
    import concourse.bacc as bacc
    from concourse.bass_utils import run_bass_kernel_spmd

    nc = bacc.Bacc("TRN2", target_bir_lowering=False, num_devices=1)
    arrays = {}

    def dram(name, a):
        arrays[name] = np.ascontiguousarray(a)
        return nc.dram_tensor(name, a.shape, mybir.dt.from_np(a.dtype), kind="ExternalInput").ap()

    fields = inputs["ids"].shape[1]
    z_units = inputs["L0_rec_inner_w"].shape[0]
    ids = dram("ids", inputs["ids"])
    tables = [dram(f"tbl_{f}", inputs[f"tbl_{f}"]) for f in range(fields)]
    w_inner = dram("w_inner", inputs["L0_rec_inner_w"].T)
    dense = dram("dense", inputs["dense_ctx"].T)
    w1z = dram("w1z", inputs["W_top1"][:z_units])
    w1d = dram("w1d", inputs["W_top1"][z_units:])
    b1 = dram("b1", inputs["b_top1"].reshape(-1, P).T)
    w2 = dram("w2", inputs["W_top2"])
    b2 = dram("b2", inputs["b_top2"].reshape(-1, P).T)
    w3 = dram("w3", inputs["W_top3"].reshape(-1, P).T)
    out = nc.dram_tensor("out", (inputs["ids"].shape[0], 1), F32, kind="ExternalOutput").ap()
    dlrm_tower(nc, ids, tables, w_inner, dense, w1z, w1d, b1, w2, b2, w3, out)
    r = run_bass_kernel_spmd(nc, [arrays], core_ids=[0])
    return r.results[0]["out"]
```

```python
from contextlib import ExitStack

import concourse.bass as bass
from concourse import mybir

F32 = mybir.dt.float32
BF16 = mybir.dt.bfloat16
FP16 = mybir.dt.float16
I32 = mybir.dt.int32
ALU = mybir.AluOpType
ACT = mybir.ActivationFunctionType
AX = mybir.AxisListType

P = 128
PARTS = 3
BANK = 512
CHUNK_E = 8
QUARTERS = 4
ROWS = 125
SELECTED = 14
AHEAD = 10
MADE_AHEAD = 2
HIGH_AT, LOW_AT = 3, 4
LAYER1_AT, LAYER2_AT, LAYER3_AT = 2, 4, 6


def field_order(vocab):
    by_size = sorted(range(len(vocab)), key=lambda f: (vocab[f], f))
    return by_size[:SELECTED] + sorted(by_size[SELECTED:])


def at_least(engine, sem, value):
    if not (isinstance(value, int) and value <= 0):
        engine.wait_ge(sem, value)


def dlrm_tower(nc, ids, ids_by_field, tables, w_inner, dense, w1z, w1d, b1, w2, b2, w3, out):
    B, F = ids.shape
    E = tables[0].shape[1]
    U = w_inner.shape[1]
    KD = dense.shape[0]
    H1 = w1z.shape[1]
    H2 = w2.shape[1]
    M1, M2 = H1 // P, H2 // P
    TILES = B // P
    PAIRS = TILES // 2
    PB = 2 * P
    K = PARTS * F
    CHUNKS = E // CHUNK_E
    CCOLS = CHUNK_E * P
    CQ = CHUNKS // QUARTERS
    EQ = E // QUARTERS
    NS = SELECTED
    NG = F - NS
    GROUPS = NS // 2
    blocks = [tables[j].shape[0] // ROWS for j in range(NS)]
    C = blocks[0]
    assert U == P and K <= P and B % PB == 0 and M1 * PB == 2 * BANK and M2 * PB == BANK
    assert all(tables[j].shape[0] % ROWS == 0 and tables[j].shape[0] <= 2048 for j in range(NS))
    assert all(c == C for c in blocks) and GROUPS == CHUNKS - 1

    with ExitStack() as ctx:
        def sb(name, shape, dt):
            return ctx.enter_context(nc.sbuf_tensor(name, shape, dt))

        def sem(name):
            return ctx.enter_context(nc.semaphore(name))

        def sems(name, n=2):
            return [sem(f"{name}{k}") for k in range(n)]

        scratch = nc.dram_tensor("ids_fp16", [TILES, NS, P], FP16, kind="Internal").ap()

        idx = sb("idx", [P, 2, F], I32)
        emb = sb("emb", [P, 2, NG, E], F32)
        split = sb("split", [P, 2, E, P], BF16)
        moved = sb("moved", [P, 2, E, P], BF16)
        squares = sb("squares", [U, 2, EQ + 1, P], F32)
        table_parts = sb("table_parts", [ROWS, NS, C, PARTS, E], BF16)
        ids_all = sb("ids_all", [P, 2, NS, P], FP16)
        row_int = sb("row_int", [ROWS, C], I32)
        row_of = sb("row_of", [ROWS, C, P], FP16)
        onehot = sb("onehot", [ROWS, 4, 2, C, P], BF16)
        z = sb("z", [U, PB], F32)
        w_rep = sb("w_rep", [K, U], F32)
        w_parts = sb("w_parts", [K, PARTS, U], BF16)
        w1z_sb = sb("w1z_sb", [U, H1], F32)
        w1d_sb = sb("w1d_sb", [KD, H1], F32)
        w2_sb = sb("w2_sb", [P, M1, H2], F32)
        w3_sb = sb("w3_sb", [P, M2], F32)
        b1_sb = sb("b1_sb", [P, M1], F32)
        b2_sb = sb("b2_sb", [P, M2], F32)
        dense_sb = sb("dense_sb", [KD, B], F32)
        h1 = sb("h1", [P, M1, PB], F32)
        h2 = sb("h2", [P, M2, PB], F32)
        y_sb = sb("y_sb", [1, B], F32)

        stage = moved[0:ROWS, :, :, :].rearrange("p k e b -> p (k e b)").bitcast(F32)[:, 0:NS * C * E].rearrange(
            "p (j c e) -> p j c e", j=NS, c=C)
        ids_int = split[0:NS, 0, :, :].rearrange("p e b -> p (e b)").bitcast(I32)[:, 0:B]
        ids_half = split[0:NS, 1, :, :].rearrange("p e b -> p (e b)").bitcast(FP16)[:, 0:B]

        delta = ctx.enter_context(nc.psum_tensor("delta", [P, 2, CCOLS], F32))
        chosen = ctx.enter_context(nc.psum_tensor("chosen", [P, 2, BANK], F32))
        hid = ctx.enter_context(nc.psum_tensor("hid", [P, 2 * BANK], F32))
        hid2 = hid[:, 0:BANK]
        yps = hid[:, BANK:2 * BANK]

        ids_ready = sems("ids_ready")
        ids_int_ready = sem("ids_int_ready")
        ids_half_ready = sem("ids_half_ready")
        ids_scratched = sem("ids_scratched")
        ids_all_ready = sems("ids_all_ready")
        gathered = sems("gathered")
        transposed = sems("transposed")
        rows_counted = sem("rows_counted")
        row_of_ready = sem("row_of_ready")
        table_loaded = sems("table_loaded", GROUPS)
        table_high = sem("table_high")
        table_rest = sem("table_rest")
        table_mid = sem("table_mid")
        table_low = sem("table_low")
        onehot_ready = sem("onehot_ready")
        chosen_ready = sem("chosen_ready")
        chosen_placed = sem("chosen_placed")
        pad_zero = sem("pad_zero")
        w_loaded = sem("w_loaded")
        mlp_loaded = sem("mlp_loaded")
        w_step = sem("w_step")
        high_ready = sem("high_ready")
        rest_ready = sem("rest_ready")
        mid_ready = sem("mid_ready")
        low_ready = sem("low_ready")
        delta_ready = sem("delta_ready")
        squared = sem("squared")
        reduced = sem("reduced")
        hid1_ready = sem("hid1_ready")
        h1_ready = sem("h1_ready")
        hid2_ready = sem("hid2_ready")
        h2_ready = sem("h2_ready")
        y_ready = sem("y_ready")
        y_free = sem("y_free")
        stored = sem("stored")
        gather_gate = sem("gather_gate")
        sync_gate = sem("sync_gate")

        MLP_LOADS = 7
        MAIN = ROWS - ROWS % 16

        block = ctx.enter_context(nc.Block())

        def tile_after(q, k, n):
            return q + (k + n) // 2, (k + n) % 2

        def turn_ahead(q, k, c, n, last):
            d, g = (c + n) // CHUNKS, (c + n) % CHUNKS
            if g == GROUPS or (last and k + d > 1):
                return None
            return (*tile_after(q, k, d), g)

        @block.sync
        def _(sp):
            def load_ids(q, k):
                sp.dma_start(idx[:, k, :], ids[bass.ds(q * PB + k * P, P), :]).then_inc(ids_ready[k], 16)

            def load_ids_all(q, k):
                src = scratch[bass.ds(q * 2 + k, 1), :, :].rearrange("t j b -> (t j b)")
                sp.dma_start(ids_all[:, k, :, :].rearrange("p j b -> p (j b)"),
                             src.partition_broadcast(P)).then_inc(ids_all_ready[k], 16)

            def transpose_tile(q, k):
                sp.wait_ge(low_ready, 2 * q + k + 1)
                sp.sem_inc(sync_gate, 1)
                sp.wait_ge(chosen_placed, (2 * q + k + 1) * GROUPS)
                sp.sem_inc(sync_gate, 1)
                at_least(sp, delta_ready, (2 * q + k - 1) * CHUNKS)
                sp.sem_inc(sync_gate, 1)
                sp.dma_start_transpose(moved[:, k, :, :], split[:, k, :, :].rearrange("b e r -> b (e r)")
                                       ).then_inc(transposed[k], 16)

            def refill(q, k):
                sp.wait_ge(gathered[k], (q + 1) * (16 * NG))
                sp.sem_inc(sync_gate, 1)
                sp.wait_ge(onehot_ready, (2 * q + k + 1) * GROUPS)
                sp.sem_inc(sync_gate, 1)
                load_ids(q + 1, k)
                load_ids_all(q + 1, k)

            def step(q):
                for k in range(2):
                    transpose_tile(q, k)
                    refill(q, k)

            load_ids(0, 0)
            sp.dma_start(ids_int, ids_by_field[0:NS, :]).then_inc(ids_int_ready, 16)
            sp.wait_ge(ids_half_ready, 1)
            sp.dma_start(scratch.rearrange("t j b -> j t b"), ids_half.rearrange("j (t b) -> j t b", b=P)
                         ).then_inc(ids_scratched, 16)
            sp.wait_ge(ids_scratched, 16)
            for k in range(2):
                load_ids_all(0, k)
            load_ids(0, 1)
            for n in range(PARTS):
                sp.dma_start(w_rep[n * F:(n + 1) * F, :], w_inner).then_inc(w_loaded, 16)
            for dst, src in ((w1z_sb[:], w1z), (w1d_sb[:], w1d), (w2_sb[:], w2.rearrange("(k p) n -> p k n", p=P)),
                             (w3_sb[:], w3), (b1_sb[:], b1), (b2_sb[:], b2), (dense_sb[:], dense)):
                sp.dma_start(dst, src).then_inc(mlp_loaded, 16)
            sp.wait_ge(pad_zero, 1)
            step(0)
            with sp.Fori(1, PAIRS - 1) as q:
                step(q)
            for k in range(2):
                transpose_tile(PAIRS - 1, k)
            sp.wait_ge(y_free, PAIRS + 1)
            sp.dma_start(out.rearrange("b n -> n b"), y_sb[:]).then_inc(stored, 16)
            sp.wait_ge(stored, 16)

        @block.gpsimd
        def _(pool):
            def gather_pair(q):
                for k in range(2):
                    pool.wait_ge(ids_ready[k], q * 16 + 16)
                    at_least(pool, low_ready, 2 * q + k - 1)
                    pool.sem_inc(gather_gate, 1)
                    for f in range(NG):
                        nc.gpsimd.indirect_dma_start(
                            emb[:, k, f, :], None, tables[NS + f][:],
                            bass.IndirectOffsetOnAxis(ap=idx[:, k, NS + f:NS + f + 1], axis=0)
                        ).then_inc(gathered[k], 16)

            nc.gpsimd.iota(row_int[:], [[1, C]], base=0, channel_multiplier=C).then_inc(rows_counted, 1)
            gather_pair(0)
            with pool.Fori(1, PAIRS) as q:
                gather_pair(q)

        def gathered_part(k, part):
            at = part * F + NS
            return split[:, k, :, at:at + NG].rearrange("b e f -> b f e")

        @block.scalar
        def _(act):
            def split_high(q, k):
                act.wait_ge(gathered[k], q * (16 * NG) + 16 * NG)
                at_least(act, transposed[k], q * 16)
                nc.scalar.copy(gathered_part(k, 0), emb[:, k, :, :]).then_inc(high_ready, 1)

            def split_mid(q, k):
                act.wait_ge(rest_ready, 2 * q + k + 1)
                nc.scalar.copy(gathered_part(k, 1), emb[:, k, :, :]).then_inc(mid_ready, 1)

            def place_chosen(q, k, g):
                act.wait_ge(chosen_ready, (2 * q + k) * GROUPS + g + 1)
                if g == 0:
                    at_least(act, transposed[k], q * 16)
                dst = split[:, k, :, 0:K].rearrange("b e (n f) -> b f n e", n=PARTS)
                nc.scalar.copy(dst[:, 2 * g:2 * g + 2, :, :],
                               chosen[:, (k + g) % 2, 0:2 * PARTS * E].rearrange("b (j n e) -> b j n e", j=2, n=PARTS)
                               ).then_inc(chosen_placed, 1)

            def square(q, k, c):
                n = (2 * q + k) * CHUNKS + c
                act.wait_ge(delta_ready, n + 1)
                slot = c // CQ % 2
                if c % CQ == 0:
                    at_least(act, reduced, (2 * q + k) * QUARTERS + c // CQ - 1)
                e0 = c % CQ * CHUNK_E
                nc.scalar.activation(squares[:, slot, e0:e0 + CHUNK_E, :].rearrange("u e b -> u (e b)"),
                                     delta[:, c % 2, :], ACT.Square).then_inc(squared, 1)

            def relu1(q):
                act.wait_ge(hid1_ready, q + 1)
                for m in range(M1):
                    nc.scalar.activation(h1[:, m, :], hid[:, m * PB:(m + 1) * PB], ACT.Relu,
                                         bias=b1_sb[:, m:m + 1]).then_inc(h1_ready, 1)

            def relu2(q):
                act.wait_ge(hid2_ready, q + 1)
                for m in range(M2):
                    nc.scalar.activation(h2[:, m, :], hid2[:, m * PB:(m + 1) * PB], ACT.Relu,
                                         bias=b2_sb[:, m:m + 1]).then_inc(h2_ready, 1)

            def copy_y(q):
                act.wait_ge(y_ready, q + 1)
                nc.scalar.copy(y_sb[:, bass.ds(q * PB, PB)], yps[0:1, 0:PB]).then_inc(y_free, 1)

            mlp = {LAYER1_AT: relu1, LAYER2_AT: relu2, LAYER3_AT: copy_y}

            def step(q, first=False, last=False):
                for k in range(2):
                    ahead = not (last and k == 1)
                    for c in range(CHUNKS):
                        if turn := turn_ahead(q, k, c, AHEAD, last):
                            place_chosen(*turn)
                        if not first and k == 0 and c in mlp:
                            mlp[c](q - 1)
                        square(q, k, c)
                        if ahead and c == HIGH_AT:
                            split_high(*tile_after(q, k, 1))
                        if ahead and c == LOW_AT:
                            split_mid(*tile_after(q, k, 1))

            for j in range(NS):
                for rows in (slice(0, MAIN), slice(MAIN, ROWS)):
                    act.dma_start(stage[rows, j, :, :], tables[j].rearrange("(p c) e -> p c e", p=ROWS)[rows, :, :]
                                  ).then_inc(table_loaded[j // 2], 16)
            for g in range(GROUPS + 2):
                if g < GROUPS:
                    act.wait_ge(table_loaded[g], 4 * 16)
                    for j in (2 * g, 2 * g + 1):
                        last = nc.scalar.copy(table_parts[:, j, :, 0, :], stage[:, j, :, :])
                    last.then_inc(table_high, 1)
                if 0 < g <= GROUPS:
                    act.wait_ge(table_rest, g)
                    for j in (2 * g - 2, 2 * g - 1):
                        last = nc.scalar.copy(table_parts[:, j, :, 1, :], stage[:, j, :, :])
                    last.then_inc(table_mid, 1)
                if g == 2:
                    act.wait_ge(pad_zero, 1)
                if g >= 2:
                    place_chosen(0, 0, g - 2)
            split_high(0, 0)
            split_mid(0, 0)
            for n in range(CHUNKS, AHEAD):
                place_chosen(0, 1, n - CHUNKS)
            act.wait_ge(mlp_loaded, 16 * MLP_LOADS)
            act.sem_inc(y_free, 1)
            step(0, first=True)
            with act.Fori(1, PAIRS - 1) as q:
                step(q)
            step(PAIRS - 1, last=True)
            relu1(PAIRS - 1)
            relu2(PAIRS - 1)
            copy_y(PAIRS - 1)

        @block.vector
        def _(dve):
            def split_rest(q, k):
                dve.wait_ge(high_ready, 2 * q + k + 1)
                nc.vector.tensor_tensor(emb[:, k, :, :], emb[:, k, :, :], gathered_part(k, 0),
                                        ALU.subtract).then_inc(rest_ready, 1)

            def split_low(q, k):
                dve.wait_ge(mid_ready, 2 * q + k + 1)
                nc.vector.tensor_tensor(gathered_part(k, 2), emb[:, k, :, :], gathered_part(k, 1),
                                        ALU.subtract).then_inc(low_ready, 1)

            def make_onehot(q, k, g):
                n = (2 * q + k) * GROUPS + g
                if g == 0:
                    dve.wait_ge(ids_all_ready[k], q * 16 + 16)
                at_least(dve, chosen_ready, n - 2)
                for j in (2 * g, 2 * g + 1):
                    last = nc.vector.tensor_tensor(
                        onehot[:, g % 4, j % 2, :, :],
                        ids_all[0:ROWS, k, j, :].unsqueeze(1).to_broadcast([ROWS, C, P]), row_of[:], ALU.is_equal)
                last.then_inc(onehot_ready, 1)

            def reduce_quarter(q, k, r, first=False):
                n = (2 * q + k) * QUARTERS + r
                dve.wait_ge(squared, (2 * q + k) * CHUNKS + (r + 1) * CQ)
                at_least(dve, reduced, n)
                if r == QUARTERS - 1:
                    if not first and k == 0:
                        dve.wait_ge(hid1_ready, q)
                    dst = z[:, k * P:(k + 1) * P]
                else:
                    dst = squares[:, (r + 1) % 2, EQ, :]
                nc.vector.tensor_reduce(dst, squares[:, r % 2, 0:EQ + (r > 0), :].rearrange("u e b -> u b e"),
                                        AX.X, ALU.add).then_inc(reduced, 1)

            def step(q, first=False, last=False):
                for k in range(2):
                    ahead = not (last and k == 1)
                    for c in range(CHUNKS):
                        if turn := turn_ahead(q, k, c, AHEAD + MADE_AHEAD, last):
                            make_onehot(*turn)
                        if ahead and c == HIGH_AT:
                            split_rest(*tile_after(q, k, 1))
                        if ahead and c == LOW_AT:
                            split_low(*tile_after(q, k, 1))
                        if c % CQ == CQ - 1:
                            reduce_quarter(q, k, c // CQ, first)

            dve.wait_ge(ids_int_ready, 16)
            nc.vector.tensor_copy(ids_half, ids_int).then_inc(ids_half_ready, 1)
            dve.wait_ge(rows_counted, 1)
            nc.vector.tensor_copy(row_of[:], row_int[:].unsqueeze(2).to_broadcast([ROWS, C, P])
                                  ).then_inc(row_of_ready, 1)
            dve.wait_ge(row_of_ready, 1)
            dve.wait_ge(ids_scratched, 16)
            nc.vector.memset(split[:, :, :, K:P], 0.0).then_inc(pad_zero, 1)
            for g in range(GROUPS + 1):
                if g < GROUPS:
                    dve.wait_ge(table_high, g + 1)
                    for j in (2 * g, 2 * g + 1):
                        last = nc.vector.tensor_tensor(stage[:, j, :, :], stage[:, j, :, :],
                                                       table_parts[:, j, :, 0, :], ALU.subtract)
                    last.then_inc(table_rest, 1)
                if g > 0:
                    dve.wait_ge(table_mid, g)
                    for j in (2 * g - 2, 2 * g - 1):
                        last = nc.vector.tensor_tensor(table_parts[:, j, :, 2, :], stage[:, j, :, :],
                                                       table_parts[:, j, :, 1, :], ALU.subtract)
                    last.then_inc(table_low, 1)
                    make_onehot(0, 0, g - 1)
            dve.wait_ge(w_loaded, 16 * PARTS)
            done = 0
            for n in range(PARTS):
                nc.vector.tensor_copy(w_parts[:, n, :], w_rep[:]).then_inc(w_step, 1)
                done += 1
                if n < PARTS - 1:
                    dve.wait_ge(w_step, done)
                    nc.vector.tensor_tensor(w_rep[:], w_rep[:], w_parts[:, n, :], ALU.subtract).then_inc(w_step, 1)
                    done += 1
                    dve.wait_ge(w_step, done)
            split_rest(0, 0)
            split_low(0, 0)
            for n in range(CHUNKS, AHEAD + MADE_AHEAD):
                make_onehot(0, 1, n - CHUNKS)
            step(0, first=True)
            with dve.Fori(1, PAIRS - 1) as q:
                step(q)
            step(PAIRS - 1, last=True)

        @block.tensor
        def _(pe):
            def choose(q, k, g):
                n = (2 * q + k) * GROUPS + g
                pe.wait_ge(onehot_ready, n + 1)
                at_least(pe, chosen_placed, n - 1)
                for j in (2 * g, 2 * g + 1):
                    at = j % 2 * PARTS * E
                    for c in range(C):
                        last = nc.tensor.matmul(chosen[:, (k + g) % 2, at:at + PARTS * E], onehot[:, g % 4, j % 2, c, :],
                                                table_parts[:, j, c, :, :].rearrange("p n e -> p (n e)"),
                                                start=(c == 0), stop=(c == C - 1))
                last.then_inc(chosen_ready, 1)

            def product(q, k, c):
                n = (2 * q + k) * CHUNKS + c
                at_least(pe, squared, n - 1)
                for part in range(PARTS):
                    for h in range(CCOLS // BANK):
                        e0 = c * CHUNK_E + h * (BANK // P)
                        last = nc.tensor.matmul(delta[:, c % 2, h * BANK:(h + 1) * BANK], w_parts[:, part, :],
                                                moved[0:K, k, e0:e0 + BANK // P, :].rearrange("r e b -> r (e b)"),
                                                start=(part == 0), stop=(part == PARTS - 1))
                last.then_inc(delta_ready, 1)

            def layer1(q):
                pe.wait_ge(reduced, (q + 1) * (2 * QUARTERS))
                pe.wait_ge(y_free, q + 1)
                for m in range(M1):
                    o = hid[:, m * PB:(m + 1) * PB]
                    nc.tensor.matmul(o, w1z_sb[:, m * P:(m + 1) * P], z[:], start=True, stop=False)
                    last = nc.tensor.matmul(o, w1d_sb[:, m * P:(m + 1) * P], dense_sb[:, bass.ds(q * PB, PB)],
                                            start=False, stop=True)
                last.then_inc(hid1_ready, 1)

            def layer2(q):
                pe.wait_ge(h1_ready, q * M1 + M1)
                for m in range(M2):
                    for j in range(M1):
                        last = nc.tensor.matmul(hid2[:, m * PB:(m + 1) * PB], w2_sb[:, j, m * P:(m + 1) * P],
                                                h1[:, j, :], start=(j == 0), stop=(j == M1 - 1))
                last.then_inc(hid2_ready, 1)

            def layer3(q):
                pe.wait_ge(h2_ready, q * M2 + M2)
                for j in range(M2):
                    last = nc.tensor.matmul(yps[0:1, 0:PB], w3_sb[:, j:j + 1], h2[:, j, :],
                                            start=(j == 0), stop=(j == M2 - 1))
                last.then_inc(y_ready, 1)

            mlp = {LAYER1_AT: layer1, LAYER2_AT: layer2, LAYER3_AT: layer3}

            def step(q, first=False, last=False):
                for k in range(2):
                    for c in range(CHUNKS):
                        if turn := turn_ahead(q, k, c, AHEAD, last):
                            choose(*turn)
                        if not first and k == 0 and c in mlp:
                            mlp[c](q - 1)
                        if c == 0:
                            pe.wait_ge(transposed[k], q * 16 + 16)
                        product(q, k, c)

            for g in range(GROUPS):
                pe.wait_ge(table_low, g + 1)
                choose(0, 0, g)
            for n in range(CHUNKS, AHEAD):
                choose(0, 1, n - CHUNKS)
            pe.wait_ge(w_step, 2 * PARTS - 1)
            pe.wait_ge(mlp_loaded, 16 * MLP_LOADS)
            step(0, first=True)
            with pe.Fori(1, PAIRS - 1) as q:
                step(q)
            step(PAIRS - 1, last=True)
            layer1(PAIRS - 1)
            layer2(PAIRS - 1)
            layer3(PAIRS - 1)


def kernel(**inputs):
    import numpy as np
    import concourse.bacc as bacc
    from concourse.bass_utils import run_bass_kernel_spmd

    nc = bacc.Bacc("TRN2", target_bir_lowering=False, num_devices=1)
    arrays = {}

    def dram(name, a):
        arrays[name] = np.ascontiguousarray(a)
        return nc.dram_tensor(name, a.shape, mybir.dt.from_np(a.dtype), kind="ExternalInput").ap()

    fields = inputs["ids"].shape[1]
    order = field_order([inputs[f"tbl_{f}"].shape[0] for f in range(fields)])
    z_units = inputs["L0_rec_inner_w"].shape[0]
    ids = dram("ids", inputs["ids"][:, order])
    ids_by_field = dram("ids_by_field", inputs["ids"][:, order].T)
    tables = [dram(f"tbl_{f}", inputs[f"tbl_{f}"]) for f in order]
    w_inner = dram("w_inner", inputs["L0_rec_inner_w"][:, order].T)
    dense = dram("dense", inputs["dense_ctx"].T)
    w1z = dram("w1z", inputs["W_top1"][:z_units])
    w1d = dram("w1d", inputs["W_top1"][z_units:])
    b1 = dram("b1", inputs["b_top1"].reshape(-1, P).T)
    w2 = dram("w2", inputs["W_top2"])
    b2 = dram("b2", inputs["b_top2"].reshape(-1, P).T)
    w3 = dram("w3", inputs["W_top3"].reshape(-1, P).T)
    out = nc.dram_tensor("out", (inputs["ids"].shape[0], 1), F32, kind="ExternalOutput").ap()
    dlrm_tower(nc, ids, ids_by_field, tables, w_inner, dense, w1z, w1d, b1, w2, b2, w3, out)
    r = run_bass_kernel_spmd(nc, [arrays], core_ids=[0])
    return r.results[0]["out"]
```

```python
from contextlib import ExitStack

import concourse.bass as bass
from concourse import mybir

F32 = mybir.dt.float32
BF16 = mybir.dt.bfloat16
FP16 = mybir.dt.float16
I32 = mybir.dt.int32
ALU = mybir.AluOpType
ACT = mybir.ActivationFunctionType
AX = mybir.AxisListType

P = 128
PARTS = 3
BANK = 512
CHUNK_E = 8
QUARTERS = 4
HALVES = 2
ROWS = 125
SELECTED = 16
AHEAD = 13
MADE_AHEAD = 3
PLACE_BEHIND = 3
FIRST_SPLIT_AT = 6
HIGH_AT, REST_AT, MID_AT, LOW_AT = 0, 1, 1, 2
LAYER1_AT, LAYER2_AT, LAYER3_AT = 3, 5, 7
STACK = [(0, 0), (0, 1), (0, 2), (1, 0), (1, 1), (1, 2), (2, 0), (2, 1)]


def field_order(vocab):
    by_size = sorted(range(len(vocab)), key=lambda f: (vocab[f], f))
    return by_size[:SELECTED] + sorted(by_size[SELECTED:])


def at_least(engine, sem, value):
    if not (isinstance(value, int) and value <= 0):
        engine.wait_ge(sem, value)


def dlrm_tower(nc, ids, ids_by_field, selected, tables, w_inner, dense, w1z, w1d, b1, w2, b2, w3, out):
    B, F = ids.shape
    E = tables[0].shape[1]
    U = w_inner.shape[1]
    KD = dense.shape[0]
    H1 = w1z.shape[1]
    H2 = w2.shape[1]
    M1, M2 = H1 // P, H2 // P
    TILES = B // P
    PAIRS = TILES // 2
    PB = 2 * P
    CUTS = P // KD
    DC, WC = B // CUTS, H1 // CUTS
    BM = BANK // PB
    K = PARTS * F
    CHUNKS = E // CHUNK_E
    CCOLS = CHUNK_E * P
    CQ = CHUNKS // QUARTERS
    EQ = E // QUARTERS
    NS = SELECTED
    NG = F - NS
    GROUPS = NS // 2
    group_tables = [t[j:j + 2] for t in selected for j in range(0, t.shape[0], 2)]
    blocks = [t.shape[1] // ROWS for t in group_tables]
    block_at = [2 * sum(blocks[:g]) for g in range(GROUPS + 1)]
    kinds = sorted(set(blocks))
    CMAX = max(blocks)
    MADE_SLOTS = 4
    BEFORE = MADE_SLOTS - (GROUPS % MADE_SLOTS > 0)
    assert P % KD == 0 and len(STACK) * KD == P
    assert U == P and K <= P and B % PB == 0 and M1 * PB == 2 * BANK and M2 * PB == BANK
    assert all(t.shape[0] == 2 and t.shape[1] % ROWS == 0 and t.shape[1] <= 2048 for t in group_tables)
    assert len(group_tables) == GROUPS and CHUNKS - 1 <= GROUPS <= CHUNKS

    with ExitStack() as ctx:
        def sb(name, shape, dt):
            return ctx.enter_context(nc.sbuf_tensor(name, shape, dt))

        def sem(name):
            return ctx.enter_context(nc.semaphore(name))

        def sems(name, n=2):
            return [sem(f"{name}{k}") for k in range(n)]

        scratch = nc.dram_tensor("ids_fp16", [TILES, NS, P], FP16, kind="Internal").ap()

        flat_parts = nc.dram_tensor("flat_parts", [P, PARTS, DC + WC], BF16, kind="Internal").ap()

        idx = sb("idx", [P, 2, F], I32)
        emb = sb("emb", [P, 2, NG, E], F32)
        split = sb("split", [P, 2, E, P], BF16)
        moved = sb("moved", [P, 2, E, P], BF16)
        squares = sb("squares", [U, 2, EQ + 1, P], F32)
        table_parts = sb("table_parts", [ROWS, block_at[GROUPS], PARTS, E], BF16)
        ids_all = sb("ids_all", [P, 2, NS, P], FP16)
        row_int = sb("row_int", [ROWS, len(kinds), CMAX], I32)
        row_of = sb("row_of", [ROWS, len(kinds), CMAX, P], FP16)
        onehot = sb("onehot", [ROWS, MADE_SLOTS, 2, CMAX, P], BF16)
        z = sb("z", [U, PB], F32)
        w_rep = sb("w_rep", [K, U], F32)
        w_parts = sb("w_parts", [K, PARTS, U], BF16)
        w1z_sb = sb("w1z_sb", [U, H1], F32)
        w1d_stack = sb("w1d_stack", [P, H1], BF16)
        w2_sb = sb("w2_sb", [P, M1, H2], F32)
        w3_sb = sb("w3_sb", [P, M2], F32)
        b1_sb = sb("b1_sb", [P, M1], F32)
        b2_sb = sb("b2_sb", [P, M2], F32)
        dense_stack = sb("dense_stack", [P, B], BF16)
        h1 = sb("h1", [P, M1, PB], F32)
        h2 = sb("h2", [P, M2, PB], F32)
        y_sb = sb("y_sb", [1, B], F32)

        stage_a = moved[0:ROWS, :, :, :].rearrange("p k e b -> p (k e b)").bitcast(F32).rearrange(
            "p (n e) -> p n e", e=E)
        stage_b = squares[0:ROWS, :, :, :].rearrange("p k e b -> p (k e b)").rearrange("p (n e) -> p n e", e=E)
        in_a = sum(block_at[g + 1] <= stage_a.shape[1] for g in range(GROUPS))

        flat = h1[:].rearrange("p m b -> p (m b)")[:, 0:DC + WC]
        flat_split = h1[:].rearrange("p m b -> p (m b)").bitcast(BF16)[
            :, 2 * (DC + WC):(2 + PARTS) * (DC + WC)].rearrange("p (n x) -> p n x", n=PARTS)

        def stage(g, n=1):
            if g < in_a:
                return stage_a[:, block_at[g]:block_at[g + n], :]
            return stage_b[:, block_at[g] - block_at[in_a]:block_at[g + n] - block_at[in_a], :]

        ids_int = onehot[0:NS].rearrange("p s j c b -> p (s j c b)").bitcast(I32)[:, 0:B]
        ids_half = onehot[0:NS].rearrange("p s j c b -> p (s j c b)").bitcast(FP16)[:, 2 * B:3 * B]

        delta = ctx.enter_context(nc.psum_tensor("delta", [P, 2, CCOLS], F32))
        chosen = ctx.enter_context(nc.psum_tensor("chosen", [P, 2, BANK], F32))
        hid = ctx.enter_context(nc.psum_tensor("hid", [P, 2 * BANK], F32))
        hid2 = hid[:, 0:BANK]
        yps = hid[:, BANK:2 * BANK]

        ids_ready = sems("ids_ready")
        ids_int_ready = sem("ids_int_ready")
        ids_half_ready = sem("ids_half_ready")
        ids_scratched = sem("ids_scratched")
        ids_all_ready = sems("ids_all_ready")
        gathered = sems("gathered")
        transposed = [sems(f"transposed{h}_") for h in range(HALVES)]
        rows_counted = sem("rows_counted")
        row_of_ready = sem("row_of_ready")
        table_loaded = sems("table_loaded", GROUPS)
        table_high = sem("table_high")
        table_rest = sem("table_rest")
        table_mid = sem("table_mid")
        table_low = sem("table_low")
        onehot_ready = sem("onehot_ready")
        chosen_ready = sem("chosen_ready")
        chosen_placed = sem("chosen_placed")
        pad_zero = sem("pad_zero")
        w_loaded = sem("w_loaded")
        mlp_loaded = sem("mlp_loaded")
        flat_loaded = sem("flat_loaded")
        flat_step = sem("flat_step")
        flat_stored = sem("flat_stored")
        stacked = sem("stacked")
        w_step = sem("w_step")
        high_ready = sem("high_ready")
        rest_ready = sem("rest_ready")
        mid_ready = sem("mid_ready")
        low_ready = sem("low_ready")
        delta_ready = sem("delta_ready")
        squared = sem("squared")
        reduced = sem("reduced")
        hid1_ready = sem("hid1_ready")
        h1_ready = sem("h1_ready")
        hid2_ready = sem("hid2_ready")
        h2_ready = sem("h2_ready")
        y_ready = sem("y_ready")
        y_free = sem("y_free")
        stored = sem("stored")
        gather_gate = sem("gather_gate")
        sync_gate = sem("sync_gate")

        MLP_LOADS = 5
        cuts = {0, 1, 2, 4, in_a, GROUPS} | {sum(t.shape[0] // 2 for t in selected[:n]) for n in range(len(selected))}
        cuts = sorted(cuts)
        load_sets = [(a, b - a) for a, b in zip(cuts, cuts[1:])]
        set_starts = [a for a, _ in load_sets]
        MAIN = ROWS - ROWS % 16

        def set_tables(g, n):
            for t in selected:
                if g < t.shape[0] // 2:
                    return t[2 * g:2 * (g + n)]
                g -= t.shape[0] // 2

        def load_tables(engine, sets):
            for g, n in sets:
                for rows in (slice(0, MAIN), slice(MAIN, ROWS)):
                    engine.dma_start(stage(g, n)[rows].rearrange("p (j c) e -> p j (c e)", j=2 * n),
                                     set_tables(g, n).rearrange("j (p c) e -> p j (c e)", p=ROWS)[rows]
                                     ).then_inc(table_loaded[g], 16)

        FLAT_STEPS = 2 * PARTS - 1

        block = ctx.enter_context(nc.Block())

        def tile_after(q, k, n):
            return q + (k + n) // 2, (k + n) % 2

        def mlp_run(q, k):
            return (q, 0, PB) if k is None else (q + k, k * P, P)

        def bank_of(k, g):
            return (k * GROUPS + g) % 2

        def turn_ahead(q, k, c, n, last):
            d, g = (c + n) // CHUNKS, (c + n) % CHUNKS
            if g >= GROUPS or (last and k + d > 1):
                return None
            return (*tile_after(q, k, d), g)

        @block.sync
        def _(sp):
            def load_ids(q, k):
                sp.dma_start(idx[:, k, :], ids[bass.ds(q * PB + k * P, P), :]).then_inc(ids_ready[k], 16)

            def load_ids_all(q, k):
                src = scratch[bass.ds(q * 2 + k, 1), :, :].rearrange("t j b -> (t j b)")
                sp.dma_start(ids_all[:, k, :, :].rearrange("p j b -> p (j b)"),
                             src.partition_broadcast(P)).then_inc(ids_all_ready[k], 16)

            def transpose_tile(q, k):
                sp.wait_ge(low_ready, 2 * q + k + 1)
                sp.sem_inc(sync_gate, 1)
                sp.wait_ge(chosen_placed, (2 * q + k + 1) * GROUPS)
                sp.sem_inc(sync_gate, 1)
                at_least(sp, delta_ready, (2 * q + k - 1) * CHUNKS)
                sp.sem_inc(sync_gate, 1)
                for h in range(HALVES):
                    half = slice(h * E // HALVES, (h + 1) * E // HALVES)
                    sp.dma_start_transpose(moved[:, k, half, :], split[:, k, half, :].rearrange("b e r -> b (e r)")
                                           ).then_inc(transposed[h][k], 16)

            def refill_ids(q, k):
                sp.wait_ge(gathered[k], (q + 1) * (16 * NG))
                sp.sem_inc(sync_gate, 1)
                load_ids(q + 1, k)

            def refill_ids_all(q, k):
                sp.wait_ge(onehot_ready, (2 * q + k + 1) * GROUPS)
                sp.sem_inc(sync_gate, 1)
                load_ids_all(q + 1, k)

            def stack_dense():
                sp.wait_ge(flat_step, FLAT_STEPS)
                sp.dma_start(flat_parts, flat_split).then_inc(flat_stored, 16)
                sp.wait_ge(flat_stored, 16)
                parts = flat_parts.rearrange("(d c) n x -> d n c x", c=CUTS)
                for n, (wp, dp) in enumerate(STACK):
                    rows = slice(n * KD, (n + 1) * KD)
                    sp.dma_start(dense_stack[rows, :].rearrange("d (c x) -> d c x", c=CUTS), parts[:, dp, :, 0:DC]
                                 ).then_inc(stacked, 16)
                    sp.dma_start(w1d_stack[rows, :].rearrange("d (c x) -> d c x", c=CUTS), parts[:, wp, :, DC:DC + WC]
                                 ).then_inc(stacked, 16)

            def step(q, first=False):
                for k in range(2):
                    refill_ids(q, k)
                    transpose_tile(q, k)
                    refill_ids_all(q, k)
                    if first and k == 0:
                        stack_dense()

            load_ids(0, 0)
            sp.dma_start(ids_int, ids_by_field[0:NS, :]).then_inc(ids_int_ready, 16)
            load_tables(sp, load_sets[2:3])
            sp.wait_ge(ids_half_ready, 1)
            sp.dma_start(scratch.rearrange("t j b -> j t b"), ids_half.rearrange("j (t b) -> j t b", b=P)
                         ).then_inc(ids_scratched, 16)
            sp.wait_ge(ids_scratched, 16)
            load_ids_all(0, 0)
            load_tables(sp, load_sets[3:])
            load_ids(0, 1)
            load_ids_all(0, 1)
            for n in range(PARTS):
                sp.dma_start(w_rep[n * F:(n + 1) * F, :], w_inner).then_inc(w_loaded, 16)
            for dst, src in ((w1z_sb[:], w1z), (w2_sb[:], w2.rearrange("(k p) n -> p k n", p=P)),
                             (w3_sb[:], w3), (b1_sb[:], b1), (b2_sb[:], b2)):
                sp.dma_start(dst, src).then_inc(mlp_loaded, 16)
            for dst, src in ((flat[:, 0:DC], dense), (flat[:, DC:DC + WC], w1d)):
                sp.dma_start(dst, src.rearrange("d (c x) -> (d c) x", c=CUTS)).then_inc(flat_loaded, 16)
            sp.wait_ge(pad_zero, 1)
            step(0, first=True)
            with sp.Fori(1, PAIRS - 1) as q:
                step(q)
            for k in range(2):
                transpose_tile(PAIRS - 1, k)
            sp.wait_ge(y_free, PAIRS + 2)
            sp.dma_start(out.rearrange("b n -> n b"), y_sb[:]).then_inc(stored, 16)
            sp.wait_ge(stored, 16)

        @block.gpsimd
        def _(pool):
            def gather_pair(q):
                for k in range(2):
                    pool.wait_ge(ids_ready[k], q * 16 + 16)
                    at_least(pool, low_ready, 2 * q + k - 1)
                    pool.sem_inc(gather_gate, 1)
                    for f in range(NG):
                        nc.gpsimd.indirect_dma_start(
                            emb[:, k, f, :], None, tables[f][:],
                            bass.IndirectOffsetOnAxis(ap=idx[:, k, NS + f:NS + f + 1], axis=0)
                        ).then_inc(gathered[k], 16)

            for n, c in enumerate(kinds):
                nc.gpsimd.iota(row_int[:, n, 0:c], [[1, c]], base=0, channel_multiplier=c).then_inc(rows_counted, 1)
            gather_pair(0)
            with pool.Fori(1, PAIRS) as q:
                gather_pair(q)

        def gathered_part(k, part):
            at = part * F + NS
            return split[:, k, :, at:at + NG].rearrange("b e f -> b f e")

        @block.scalar
        def _(act):
            def split_high(q, k):
                act.wait_ge(gathered[k], q * (16 * NG) + 16 * NG)
                for h in range(HALVES):
                    at_least(act, transposed[h][k], q * 16)
                nc.scalar.copy(gathered_part(k, 0), emb[:, k, :, :]).then_inc(high_ready, 1)

            def split_mid(q, k):
                act.wait_ge(rest_ready, 2 * q + k + 1)
                nc.scalar.copy(gathered_part(k, 1), emb[:, k, :, :]).then_inc(mid_ready, 1)

            def place_chosen(q, k, g):
                act.wait_ge(chosen_ready, (2 * q + k) * GROUPS + g + 1)
                if g == 0:
                    for h in range(HALVES):
                        at_least(act, transposed[h][k], q * 16)
                dst = split[:, k, :, 0:K].rearrange("b e (n f) -> b f n e", n=PARTS)
                nc.scalar.copy(dst[:, 2 * g:2 * g + 2, :, :],
                               chosen[:, bank_of(k, g), 0:2 * PARTS * E].rearrange("b (j n e) -> b j n e", j=2, n=PARTS)
                               ).then_inc(chosen_placed, 1)

            def square(q, k, c):
                n = (2 * q + k) * CHUNKS + c
                act.wait_ge(delta_ready, n + 1)
                slot = c // CQ % 2
                if c % CQ == 0:
                    at_least(act, reduced, (2 * q + k) * QUARTERS + c // CQ - 1)
                e0 = c % CQ * CHUNK_E
                nc.scalar.activation(squares[:, slot, e0:e0 + CHUNK_E, :].rearrange("u e b -> u (e b)"),
                                     delta[:, c % 2, :], ACT.Square).then_inc(squared, 1)

            def relu1(q, k=None):
                r, _, w = mlp_run(q, k)
                for m in range(M1):
                    if m % BM == 0:
                        act.wait_ge(hid1_ready, r * (M1 // BM) + m // BM + 1)
                    nc.scalar.activation(h1[:, m, 0:w], hid[:, m * PB:m * PB + w], ACT.Relu,
                                         bias=b1_sb[:, m:m + 1]).then_inc(h1_ready, 1)

            def relu2(q, k=None):
                r, _, w = mlp_run(q, k)
                act.wait_ge(hid2_ready, r + 1)
                for m in range(M2):
                    nc.scalar.activation(h2[:, m, 0:w], hid2[:, m * PB:m * PB + w], ACT.Relu,
                                         bias=b2_sb[:, m:m + 1]).then_inc(h2_ready, 1)

            def copy_y(q, k=None):
                r, at, w = mlp_run(q, k)
                act.wait_ge(y_ready, r + 1)
                nc.scalar.copy(y_sb[:, bass.ds(q * PB + at, w)], yps[0:1, 0:w]).then_inc(y_free, 1)

            mlp = {LAYER1_AT: relu1, LAYER2_AT: relu2, LAYER3_AT: copy_y}

            def step(q, first=False, last=False):
                for k in range(2):
                    ahead = not (last and k == 1)
                    for c in range(CHUNKS):
                        if turn := turn_ahead(q, k, c, AHEAD, last):
                            place_chosen(*turn)
                        if not first and k == 0 and c in mlp:
                            mlp[c](q - 1)
                        if last and k == 1 and c in mlp:
                            mlp[c](q, 0)
                        square(q, k, c)
                        if ahead and c == HIGH_AT:
                            split_high(*tile_after(q, k, 1))
                        if ahead and c == MID_AT:
                            split_mid(*tile_after(q, k, 1))

            load_tables(act, load_sets[:2])
            for g in range(GROUPS + PLACE_BEHIND):
                if g < GROUPS:
                    if g in set_starts:
                        act.wait_ge(table_loaded[g], 2 * 16)
                    nc.scalar.copy(table_parts[:, block_at[g]:block_at[g + 1], 0, :], stage(g)).then_inc(table_high, 1)
                if 0 < g <= GROUPS:
                    act.wait_ge(table_rest, g)
                    nc.scalar.copy(table_parts[:, block_at[g - 1]:block_at[g], 1, :], stage(g - 1)
                                   ).then_inc(table_mid, 1)
                if g == PLACE_BEHIND:
                    act.wait_ge(pad_zero, 1)
                if g >= PLACE_BEHIND:
                    place_chosen(0, 0, g - PLACE_BEHIND)
                if g == FIRST_SPLIT_AT:
                    split_high(0, 0)
                if g == GROUPS:
                    split_mid(0, 0)
            for n in range(CHUNKS, AHEAD):
                if turn := turn_ahead(0, 0, 0, n, False):
                    place_chosen(*turn)
            act.wait_ge(mlp_loaded, 16 * MLP_LOADS)
            act.sem_inc(y_free, 1)
            step(0, first=True)
            with act.Fori(1, PAIRS - 1) as q:
                step(q)
            step(PAIRS - 1, last=True)
            relu1(PAIRS - 1, 1)
            relu2(PAIRS - 1, 1)
            copy_y(PAIRS - 1, 1)

        @block.vector
        def _(dve):
            def split_rest(q, k):
                dve.wait_ge(high_ready, 2 * q + k + 1)
                nc.vector.tensor_tensor(emb[:, k, :, :], emb[:, k, :, :], gathered_part(k, 0),
                                        ALU.subtract).then_inc(rest_ready, 1)

            def split_low(q, k):
                dve.wait_ge(mid_ready, 2 * q + k + 1)
                nc.vector.tensor_tensor(gathered_part(k, 2), emb[:, k, :, :], gathered_part(k, 1),
                                        ALU.subtract).then_inc(low_ready, 1)

            def make_onehot(q, k, g):
                n = (2 * q + k) * GROUPS + g
                if g == 0:
                    dve.wait_ge(ids_all_ready[k], q * 16 + 16)
                at_least(dve, chosen_ready, n + 1 - BEFORE)
                c = blocks[g]
                for j in range(2):
                    last = nc.vector.tensor_tensor(
                        onehot[:, g % MADE_SLOTS, j, 0:c, :],
                        ids_all[0:ROWS, k, 2 * g + j, :].unsqueeze(1).to_broadcast([ROWS, c, P]),
                        row_of[:, kinds.index(c), 0:c, :], ALU.is_equal)
                last.then_inc(onehot_ready, 1)

            def reduce_quarter(q, k, r, first=False):
                n = (2 * q + k) * QUARTERS + r
                dve.wait_ge(squared, (2 * q + k) * CHUNKS + (r + 1) * CQ)
                at_least(dve, reduced, n)
                if r == QUARTERS - 1:
                    if not first and k == 0:
                        dve.wait_ge(hid1_ready, q * (M1 // BM))
                    dst = z[:, k * P:(k + 1) * P]
                else:
                    dst = squares[:, (r + 1) % 2, EQ, :]
                nc.vector.tensor_reduce(dst, squares[:, r % 2, 0:EQ + (r > 0), :].rearrange("u e b -> u b e"),
                                        AX.X, ALU.add).then_inc(reduced, 1)

            def step(q, first=False, last=False):
                for k in range(2):
                    ahead = not (last and k == 1)
                    for c in range(CHUNKS):
                        if turn := turn_ahead(q, k, c, AHEAD + MADE_AHEAD, last):
                            make_onehot(*turn)
                        if ahead and c == REST_AT:
                            split_rest(*tile_after(q, k, 1))
                        if ahead and c == LOW_AT:
                            split_low(*tile_after(q, k, 1))
                        if c % CQ == CQ - 1:
                            reduce_quarter(q, k, c // CQ, first)

            nc.vector.memset(split[:, :, :, K:P], 0.0).then_inc(pad_zero, 1)
            dve.wait_ge(ids_int_ready, 16)
            nc.vector.tensor_copy(ids_half, ids_int).then_inc(ids_half_ready, 1)
            dve.wait_ge(rows_counted, len(kinds))
            for n, c in enumerate(kinds):
                nc.vector.tensor_copy(row_of[:, n, 0:c, :], row_int[:, n, 0:c].unsqueeze(2).to_broadcast([ROWS, c, P])
                                      ).then_inc(row_of_ready, 1)
            dve.wait_ge(row_of_ready, len(kinds))
            for g in range(GROUPS + 1):
                if g < GROUPS:
                    dve.wait_ge(table_high, g + 1)
                    nc.vector.tensor_tensor(stage(g), stage(g), table_parts[:, block_at[g]:block_at[g + 1], 0, :],
                                            ALU.subtract).then_inc(table_rest, 1)
                if g > 0:
                    dve.wait_ge(table_mid, g)
                    before = slice(block_at[g - 1], block_at[g])
                    nc.vector.tensor_tensor(table_parts[:, before, 2, :], stage(g - 1), table_parts[:, before, 1, :],
                                            ALU.subtract).then_inc(table_low, 1)
                    make_onehot(0, 0, g - 1)
                if g == FIRST_SPLIT_AT + 1:
                    split_rest(0, 0)
            split_low(0, 0)
            dve.wait_ge(w_loaded, 16 * PARTS)
            done = 0
            for n in range(PARTS):
                nc.vector.tensor_copy(w_parts[:, n, :], w_rep[:]).then_inc(w_step, 1)
                done += 1
                if n < PARTS - 1:
                    dve.wait_ge(w_step, done)
                    nc.vector.tensor_tensor(w_rep[:], w_rep[:], w_parts[:, n, :], ALU.subtract).then_inc(w_step, 1)
                    done += 1
                    dve.wait_ge(w_step, done)
            for n in range(CHUNKS, AHEAD + MADE_AHEAD):
                if turn := turn_ahead(0, 0, 0, n, False):
                    make_onehot(*turn)
            dve.wait_ge(flat_loaded, 16 * 2)
            done = 0
            for n in range(PARTS):
                nc.vector.tensor_copy(flat_split[:, n, :], flat).then_inc(flat_step, 1)
                done += 1
                if n < PARTS - 1:
                    dve.wait_ge(flat_step, done)
                    nc.vector.tensor_tensor(flat, flat, flat_split[:, n, :], ALU.subtract).then_inc(flat_step, 1)
                    done += 1
                    dve.wait_ge(flat_step, done)
            step(0, first=True)
            with dve.Fori(1, PAIRS - 1) as q:
                step(q)
            step(PAIRS - 1, last=True)

        @block.tensor
        def _(pe):
            def choose(q, k, g):
                n = (2 * q + k) * GROUPS + g
                pe.wait_ge(onehot_ready, n + 1)
                at_least(pe, chosen_placed, n - 1)
                for j in range(2):
                    at = j * PARTS * E
                    for c in range(blocks[g]):
                        last = nc.tensor.matmul(chosen[:, bank_of(k, g), at:at + PARTS * E],
                                                onehot[:, g % MADE_SLOTS, j, c, :],
                                                table_parts[:, block_at[g] + j * blocks[g] + c, :, :].rearrange(
                                                    "p n e -> p (n e)"),
                                                start=(c == 0), stop=(c == blocks[g] - 1))
                last.then_inc(chosen_ready, 1)

            def product(q, k, c):
                n = (2 * q + k) * CHUNKS + c
                at_least(pe, squared, n - 1)
                for part in range(PARTS):
                    for h in range(CCOLS // BANK):
                        e0 = c * CHUNK_E + h * (BANK // P)
                        last = nc.tensor.matmul(delta[:, c % 2, h * BANK:(h + 1) * BANK], w_parts[:, part, :],
                                                moved[0:K, k, e0:e0 + BANK // P, :].rearrange("r e b -> r (e b)"),
                                                start=(part == 0), stop=(part == PARTS - 1))
                last.then_inc(delta_ready, 1)

            def layer1(q, k=None):
                r, at, w = mlp_run(q, k)
                pe.wait_ge(reduced, (2 * q + 1 + (k is None or k)) * QUARTERS)
                pe.wait_ge(y_free, r + 1)
                for m in range(M1):
                    o = hid[:, m * PB:m * PB + w]
                    nc.tensor.matmul(o, w1d_stack[:, m * P:(m + 1) * P], dense_stack[:, bass.ds(q * PB + at, w)],
                                     start=True, stop=False)
                    last = nc.tensor.matmul(o, w1z_sb[:, m * P:(m + 1) * P], z[:, at:at + w], start=False, stop=True)
                    if m % BM == BM - 1:
                        last.then_inc(hid1_ready, 1)

            def layer2(q, k=None):
                r, _, w = mlp_run(q, k)
                for m in range(M2):
                    for j in range(M1):
                        if m == 0:
                            pe.wait_ge(h1_ready, r * M1 + max(j + 1, BM))
                        last = nc.tensor.matmul(hid2[:, m * PB:m * PB + w], w2_sb[:, j, m * P:(m + 1) * P],
                                                h1[:, j, 0:w], start=(j == 0), stop=(j == M1 - 1))
                last.then_inc(hid2_ready, 1)

            def layer3(q, k=None):
                r, _, w = mlp_run(q, k)
                for j in range(M2):
                    pe.wait_ge(h2_ready, r * M2 + j + 1)
                    last = nc.tensor.matmul(yps[0:1, 0:w], w3_sb[:, j:j + 1], h2[:, j, 0:w],
                                            start=(j == 0), stop=(j == M2 - 1))
                last.then_inc(y_ready, 1)

            mlp = {LAYER1_AT: layer1, LAYER2_AT: layer2, LAYER3_AT: layer3}

            def step(q, first=False, last=False):
                for k in range(2):
                    for c in range(CHUNKS):
                        if turn := turn_ahead(q, k, c, AHEAD, last):
                            choose(*turn)
                        if not first and k == 0 and c in mlp:
                            mlp[c](q - 1)
                        if last and k == 1 and c in mlp:
                            mlp[c](q, 0)
                        if c % (CHUNKS // HALVES) == 0:
                            pe.wait_ge(transposed[c // (CHUNKS // HALVES)][k], q * 16 + 16)
                        product(q, k, c)

            for g in range(GROUPS):
                pe.wait_ge(table_low, g + 1)
                choose(0, 0, g)
            for n in range(CHUNKS, AHEAD):
                if turn := turn_ahead(0, 0, 0, n, False):
                    choose(*turn)
            pe.wait_ge(w_step, 2 * PARTS - 1)
            pe.wait_ge(mlp_loaded, 16 * MLP_LOADS)
            step(0, first=True)
            pe.wait_ge(stacked, 2 * len(STACK) * 16)
            with pe.Fori(1, PAIRS - 1) as q:
                step(q)
            step(PAIRS - 1, last=True)
            layer1(PAIRS - 1, 1)
            layer2(PAIRS - 1, 1)
            layer3(PAIRS - 1, 1)


def kernel(**inputs):
    import numpy as np
    import concourse.bacc as bacc
    from concourse.bass_utils import run_bass_kernel_spmd

    nc = bacc.Bacc("TRN2", target_bir_lowering=False, num_devices=1)
    arrays = {}

    def dram(name, a):
        arrays[name] = np.ascontiguousarray(a)
        return nc.dram_tensor(name, a.shape, mybir.dt.from_np(a.dtype), kind="ExternalInput").ap()

    fields = inputs["ids"].shape[1]
    order = field_order([inputs[f"tbl_{f}"].shape[0] for f in range(fields)])
    z_units = inputs["L0_rec_inner_w"].shape[0]
    ids = dram("ids", inputs["ids"][:, order])
    ids_by_field = dram("ids_by_field", inputs["ids"][:, order].T)
    sizes = sorted({inputs[f"tbl_{f}"].shape[0] for f in order[:SELECTED]})
    selected = [dram(f"selected_{v}", np.stack([inputs[f"tbl_{f}"] for f in order[:SELECTED]
                                                if inputs[f"tbl_{f}"].shape[0] == v])) for v in sizes]
    tables = [dram(f"tbl_{f}", inputs[f"tbl_{f}"]) for f in order[SELECTED:]]
    w_inner = dram("w_inner", inputs["L0_rec_inner_w"][:, order].T)
    dense = dram("dense", inputs["dense_ctx"].T)
    w1z = dram("w1z", inputs["W_top1"][:z_units])
    w1d = dram("w1d", inputs["W_top1"][z_units:])
    b1 = dram("b1", inputs["b_top1"].reshape(-1, P).T)
    w2 = dram("w2", inputs["W_top2"])
    b2 = dram("b2", inputs["b_top2"].reshape(-1, P).T)
    w3 = dram("w3", inputs["W_top3"].reshape(-1, P).T)
    out = nc.dram_tensor("out", (inputs["ids"].shape[0], 1), F32, kind="ExternalOutput").ap()
    dlrm_tower(nc, ids, ids_by_field, selected, tables, w_inner, dense, w1z, w1d, b1, w2, b2, w3, out)
    r = run_bass_kernel_spmd(nc, [arrays], core_ids=[0])
    return r.results[0]["out"]
```
